# Optimizing a Trainium2 kernel written in Bass

```python
import numpy as np
import jax
import jax.numpy as jnp

def _softmax(x, axis=-1):
    return jax.nn.softmax(x, axis=axis)

def _gelu(x):
    return jax.nn.gelu(x, approximate=True)

def _silu(x):
    return jax.nn.silu(x)

def _sigmoid(x):
    return jax.nn.sigmoid(x)

def _layernorm(x, axis=-1, eps=1e-05):
    m = jnp.mean(x, axis=axis, keepdims=True)
    v = jnp.var(x, axis=axis, keepdims=True)
    return (x - m) / jnp.sqrt(v + eps)

def _scatter_add(tgt, idx, src, axis=0):
    return tgt.at[idx].add(src)

def _segment_sum(src, seg, n):
    return jax.ops.segment_sum(src, seg, n)
kernel_name = 'mk_flamingo_gated_d2_seqx_r4_350b77'

def setup_inputs(seed: int=0):
    np.random.seed(seed)
    _w = jnp.asarray

    def _rec_inputs():
        import jax
        import jax.numpy as jnp
        _rk = jax.random.key(seed)
        x = 0.002226 + 0.9996 * jax.random.normal(jax.random.fold_in(_rk, 1), (8, 112, 256), jnp.float32)
        _lenS = 112 - jax.random.randint(jax.random.fold_in(_rk, 7), (8,), 0, max(1, 112 // 4) + 1, jnp.int32)
        _lenS2 = 375 - jax.random.randint(jax.random.fold_in(_rk, 8), (8,), 0, max(1, 375 // 4) + 1, jnp.int32)
        _ctx_1024P = jax.random.normal(jax.random.fold_in(_rk, 11), (8, 16, 256), jnp.float32)
        _ctx_1024c = jax.random.dirichlet(jax.random.fold_in(_rk, 511), 0.3 * jnp.ones((16,), jnp.float32), (8, 375))
        _ctx_1024t = jnp.einsum('bsk,bkd->bsd', _ctx_1024c, _ctx_1024P)
        _ctx_1024t = _ctx_1024t * jax.lax.rsqrt(jnp.mean(jnp.square(_ctx_1024t)) + 1e-12) * 0.953939
        ctx_1024 = -7.10856e-05 + 0.999911 * (_ctx_1024t + 0.3 * jax.random.normal(jax.random.fold_in(_rk, 611), (8, 375, 256), jnp.float32))
        _g = jax.random.normal(jax.random.fold_in(_rk, 9001), (2, 2), jnp.float32)
        _g = jnp.sign(_g) * jnp.maximum(jnp.abs(_g), 1.0) + (_g == 0) * 1.0
        g_xattn = _g[0]
        g_ffn = _g[1]
        return (x, ctx_1024, g_xattn, g_ffn)
    x, ctx_1024, g_xattn, g_ffn = _rec_inputs()

    def _L0_xattn_setup():
        import jax, jax.numpy as jnp
        import numpy as np
        DIM = 256
        HEAD_DIM = 64
        NUM_HEADS = 8
        INNER = HEAD_DIM * NUM_HEADS
        ROT_DIM = HEAD_DIM
        ROPE_BASE = 10000.0
        EPS = 1e-05

        def layer_norm(x, g, b):
            mu = jnp.mean(x, axis=-1, keepdims=True)
            var = jnp.var(x, axis=-1, keepdims=True)
            return (x - mu) * jax.lax.rsqrt(var + EPS) * g + b

        def rope_rotate_k(k):
            n = k.shape[1]
            half = ROT_DIM // 2
            inv_freq = 1.0 / ROPE_BASE ** (jnp.arange(0, ROT_DIM, 2, dtype=jnp.float32) / ROT_DIM)
            theta = jnp.arange(n, dtype=jnp.float32)[:, None] * inv_freq[None, :]
            angles = jnp.concatenate([theta, theta], axis=-1)
            cos = jnp.cos(angles)[None, :, None, :].astype(k.dtype)
            sin = jnp.sin(angles)[None, :, None, :].astype(k.dtype)
            k_rope, k_pass = (k[..., :ROT_DIM], k[..., ROT_DIM:])
            neg_half = jnp.concatenate([-k_rope[..., half:], k_rope[..., :half]], axis=-1)
            k_rope = k_rope * cos + neg_half * sin
            return jnp.concatenate([k_rope, k_pass], axis=-1)
        key = jax.random.key(seed)
        ks = jax.random.split(key, 5)
        b, n, m = (8, 2048, 64)
        s = 1.0 / np.sqrt(DIM)
        return {'x': jax.random.normal(ks[0], (b, n, DIM), jnp.float32), 'latents': jax.random.normal(ks[1], (b, m, DIM), jnp.float32), 'gamma_x': jnp.ones((DIM,), jnp.float32), 'beta_x': jnp.zeros((DIM,), jnp.float32), 'gamma_l': jnp.ones((DIM,), jnp.float32), 'beta_l': jnp.zeros((DIM,), jnp.float32), 'Wq': jax.random.normal(ks[2], (DIM, INNER), jnp.float32) * s, 'Wkv': jax.random.normal(ks[3], (DIM, 2 * INNER), jnp.float32) * s, 'Wo': jax.random.normal(ks[4], (INNER, DIM), jnp.float32) * (1.0 / np.sqrt(INNER))}
    _L0_xattn_all = _L0_xattn_setup()
    _L0_xattn_in = {k: v for k, v in _L0_xattn_all.items() if k in ('gamma_x', 'beta_x', 'gamma_l', 'beta_l', 'Wq', 'Wkv', 'Wo')}
    del _L0_xattn_all

    def _L0_ffn_setup():
        import jax, jax.numpy as jnp
        import numpy as np
        H = 256
        I = 4 * H
        E = 8
        K = 2
        B, S = (2, 256)
        STD = 0.02 / np.sqrt(H)
        key = jax.random.key(seed)
        ks = jax.random.split(key, 8)
        x = jax.random.normal(ks[0], (B, S, H), dtype=jnp.float32)
        gate_w = jax.random.normal(ks[1], (H, E), dtype=jnp.float32) * STD
        bias = jnp.zeros((E,), dtype=jnp.float32)
        up_w = jax.random.normal(ks[2], (E, H, I), dtype=jnp.float32) * STD
        up_b = jnp.zeros((E, I), dtype=jnp.float32)
        down_w = jax.random.normal(ks[3], (E, I, H), dtype=jnp.float32) * STD
        down_b = jnp.zeros((E, H), dtype=jnp.float32)
        sw_up = jax.random.normal(ks[4], (H, I), dtype=jnp.float32) * STD
        sb_up = jnp.zeros((I,), dtype=jnp.float32)
        sw_down = jax.random.normal(ks[5], (I, H), dtype=jnp.float32) * STD
        sb_down = jnp.zeros((H,), dtype=jnp.float32)
        return {'x': x, 'gate_w': gate_w, 'bias': bias, 'up_w': up_w, 'up_b': up_b, 'down_w': down_w, 'down_b': down_b, 'sw_up': sw_up, 'sb_up': sb_up, 'sw_down': sw_down, 'sb_down': sb_down}
    _L0_ffn_all = _L0_ffn_setup()
    _L0_ffn_in = {k: v for k, v in _L0_ffn_all.items() if k in ('gate_w', 'bias', 'up_w', 'up_b', 'down_w', 'down_b', 'sw_up', 'sb_up', 'sw_down', 'sb_down')}
    del _L0_ffn_all

    def _L1_xattn_setup():
        import jax, jax.numpy as jnp
        import numpy as np
        EMBED = 256
        HEADS = 16
        HEAD_DIM = EMBED // HEADS
        key = jax.random.key(seed)
        ks = jax.random.split(key, 12)
        B, S, D = (4, 512, EMBED)
        scale = 1.0 / np.sqrt(D)
        inp = {'query': jax.random.normal(ks[0], (B, S, D), dtype=jnp.float32), 'key': jax.random.normal(ks[1], (B, S, D), dtype=jnp.float32), 'value': jax.random.normal(ks[2], (B, S, D), dtype=jnp.float32), 'Wq': jax.random.normal(ks[3], (D, D), dtype=jnp.float32) * scale, 'bq': jnp.zeros((D,), dtype=jnp.float32), 'Wk': jax.random.normal(ks[4], (D, D), dtype=jnp.float32) * scale, 'bk': jnp.zeros((D,), dtype=jnp.float32), 'Wv': jax.random.normal(ks[5], (D, D), dtype=jnp.float32) * scale, 'bv': jnp.zeros((D,), dtype=jnp.float32), 'Wo': jax.random.normal(ks[6], (D, D), dtype=jnp.float32) * scale, 'bo': jnp.zeros((D,), dtype=jnp.float32)}
        return inp
    _L1_xattn_all = _L1_xattn_setup()
    _L1_xattn_in = {k: v for k, v in _L1_xattn_all.items() if k in ('Wq', 'bq', 'Wk', 'bk', 'Wv', 'bv', 'Wo', 'bo')}
    del _L1_xattn_all

    def _L1_ffn_setup():
        import jax, jax.numpy as jnp
        import numpy as np
        HIDDEN = 256
        HEAD_DIM = 64
        N_EXPERTS = 16
        MIN_EXPERTS = 2
        B, T = (4, 512)

        def _normalize(x, axis):
            n = jnp.sqrt(jnp.sum(x * x, axis=axis, keepdims=True))
            return x / jnp.maximum(n, 1e-12)

        def _ste(x):
            hard = jax.lax.stop_gradient((x > 0).astype(x.dtype))
            return hard + x - jax.lax.stop_gradient(x)

        def _gating(hidden_states, sim_matrix, gates):
            b, t, c = hidden_states.shape
            flat = hidden_states.reshape(b * t, c)
            logits = _normalize(flat, -1) @ _normalize(sim_matrix, 0) - jax.nn.sigmoid(gates)
            gated = jax.nn.relu(logits)
            mask = _ste(gated)
            inactive = jnp.sum(mask, axis=1) == 0
            _, fb_idx = jax.lax.top_k(logits, MIN_EXPERTS)
            fb = jnp.zeros_like(mask).at[jnp.arange(b * t)[:, None], fb_idx].set(1.0)
            fb_applied = inactive[:, None] & (fb > 0)
            mask = jnp.where(fb_applied, 1.0, mask)
            masked_logits = jnp.where(mask > 0, gated, -jnp.inf)
            return jax.nn.softmax(masked_logits, axis=-1).reshape(b, t, -1)
        key = jax.random.key(seed)
        ks = jax.random.split(key, 6)
        xav_qkv = float(np.sqrt(6.0 / (HIDDEN + HEAD_DIM)))
        return {'hidden_states': jax.random.normal(ks[0], (B, T, HIDDEN), dtype=jnp.float32), 'sim_matrix': jax.random.normal(ks[1], (HIDDEN, N_EXPERTS), dtype=jnp.float32), 'gates': jnp.zeros((N_EXPERTS,), dtype=jnp.float32), 'q_proj': jax.random.uniform(ks[2], (N_EXPERTS, HIDDEN, HEAD_DIM), jnp.float32, -xav_qkv, xav_qkv), 'k_proj': jax.random.uniform(ks[3], (N_EXPERTS, HIDDEN, HEAD_DIM), jnp.float32, -xav_qkv, xav_qkv), 'v_proj': jax.random.uniform(ks[4], (N_EXPERTS, HIDDEN, HEAD_DIM), jnp.float32, -xav_qkv, xav_qkv), 'o_proj': jax.random.uniform(ks[5], (N_EXPERTS, HEAD_DIM, HIDDEN), jnp.float32, -xav_qkv, xav_qkv)}
    _L1_ffn_all = _L1_ffn_setup()
    _L1_ffn_in = {k: v for k, v in _L1_ffn_all.items() if k in ('sim_matrix', 'gates', 'q_proj', 'k_proj', 'v_proj', 'o_proj')}
    del _L1_ffn_all
    return {'x': x, 'ctx_1024': ctx_1024, 'g_xattn': g_xattn, 'g_ffn': g_ffn, 'L0_xattn_gamma_x': _L0_xattn_in['gamma_x'], 'L0_xattn_beta_x': _L0_xattn_in['beta_x'], 'L0_xattn_gamma_l': _L0_xattn_in['gamma_l'], 'L0_xattn_beta_l': _L0_xattn_in['beta_l'], 'L0_xattn_Wq': _L0_xattn_in['Wq'], 'L0_xattn_Wkv': _L0_xattn_in['Wkv'], 'L0_xattn_Wo': _L0_xattn_in['Wo'], 'L0_ffn_gate_w': _L0_ffn_in['gate_w'], 'L0_ffn_bias': _L0_ffn_in['bias'], 'L0_ffn_up_w': _L0_ffn_in['up_w'], 'L0_ffn_up_b': _L0_ffn_in['up_b'], 'L0_ffn_down_w': _L0_ffn_in['down_w'], 'L0_ffn_down_b': _L0_ffn_in['down_b'], 'L0_ffn_sw_up': _L0_ffn_in['sw_up'], 'L0_ffn_sb_up': _L0_ffn_in['sb_up'], 'L0_ffn_sw_down': _L0_ffn_in['sw_down'], 'L0_ffn_sb_down': _L0_ffn_in['sb_down'], 'L1_xattn_Wq': _L1_xattn_in['Wq'], 'L1_xattn_bq': _L1_xattn_in['bq'], 'L1_xattn_Wk': _L1_xattn_in['Wk'], 'L1_xattn_bk': _L1_xattn_in['bk'], 'L1_xattn_Wv': _L1_xattn_in['Wv'], 'L1_xattn_bv': _L1_xattn_in['bv'], 'L1_xattn_Wo': _L1_xattn_in['Wo'], 'L1_xattn_bo': _L1_xattn_in['bo'], 'L1_ffn_sim_matrix': _L1_ffn_in['sim_matrix'], 'L1_ffn_gates': _L1_ffn_in['gates'], 'L1_ffn_q_proj': _L1_ffn_in['q_proj'], 'L1_ffn_k_proj': _L1_ffn_in['k_proj'], 'L1_ffn_v_proj': _L1_ffn_in['v_proj'], 'L1_ffn_o_proj': _L1_ffn_in['o_proj']}

def reference(x, ctx_1024, g_xattn, g_ffn, L0_xattn_gamma_x, L0_xattn_beta_x, L0_xattn_gamma_l, L0_xattn_beta_l, L0_xattn_Wq, L0_xattn_Wkv, L0_xattn_Wo, L0_ffn_gate_w, L0_ffn_bias, L0_ffn_up_w, L0_ffn_up_b, L0_ffn_down_w, L0_ffn_down_b, L0_ffn_sw_up, L0_ffn_sb_up, L0_ffn_sw_down, L0_ffn_sb_down, L1_xattn_Wq, L1_xattn_bq, L1_xattn_Wk, L1_xattn_bk, L1_xattn_Wv, L1_xattn_bv, L1_xattn_Wo, L1_xattn_bo, L1_ffn_sim_matrix, L1_ffn_gates, L1_ffn_q_proj, L1_ffn_k_proj, L1_ffn_v_proj, L1_ffn_o_proj):
    import jax
    import jax.numpy as jnp

    def _L0_xattn_ref(x, latents, gamma_x, beta_x, gamma_l, beta_l, Wq, Wkv, Wo):
        import jax, jax.numpy as jnp
        import numpy as np
        DIM = 256
        HEAD_DIM = 64
        NUM_HEADS = 8
        INNER = HEAD_DIM * NUM_HEADS
        ROT_DIM = HEAD_DIM
        ROPE_BASE = 10000.0
        EPS = 1e-05

        def layer_norm(x, g, b):
            mu = jnp.mean(x, axis=-1, keepdims=True)
            var = jnp.var(x, axis=-1, keepdims=True)
            return (x - mu) * jax.lax.rsqrt(var + EPS) * g + b

        def rope_rotate_k(k):
            n = k.shape[1]
            half = ROT_DIM // 2
            inv_freq = 1.0 / ROPE_BASE ** (jnp.arange(0, ROT_DIM, 2, dtype=jnp.float32) / ROT_DIM)
            theta = jnp.arange(n, dtype=jnp.float32)[:, None] * inv_freq[None, :]
            angles = jnp.concatenate([theta, theta], axis=-1)
            cos = jnp.cos(angles)[None, :, None, :].astype(k.dtype)
            sin = jnp.sin(angles)[None, :, None, :].astype(k.dtype)
            k_rope, k_pass = (k[..., :ROT_DIM], k[..., ROT_DIM:])
            neg_half = jnp.concatenate([-k_rope[..., half:], k_rope[..., :half]], axis=-1)
            k_rope = k_rope * cos + neg_half * sin
            return jnp.concatenate([k_rope, k_pass], axis=-1)
        b, n, _ = x.shape
        m = latents.shape[1]
        h, d = (NUM_HEADS, HEAD_DIM)
        scale = d ** (-0.5)
        xn = layer_norm(x, gamma_x, beta_x)
        ln = layer_norm(latents, gamma_l, beta_l)
        q = (ln @ Wq).reshape(b, m, h, d)
        kv_x = xn @ Wkv
        k_x, v_x = (kv_x[..., :INNER], kv_x[..., INNER:])
        kv_l = ln @ Wkv
        k_l, v_l = (kv_l[..., :INNER], kv_l[..., INNER:])
        k_x = k_x.reshape(b, n, h, d)
        v_x = v_x.reshape(b, n, h, d)
        k_x = rope_rotate_k(k_x)
        q = jnp.transpose(q, (0, 2, 1, 3)) * scale
        k_x = jnp.transpose(k_x, (0, 2, 1, 3))
        v_x = jnp.transpose(v_x, (0, 2, 1, 3))
        k_l = jnp.transpose(k_l.reshape(b, m, h, d), (0, 2, 1, 3))
        v_l = jnp.transpose(v_l.reshape(b, m, h, d), (0, 2, 1, 3))
        k = jnp.concatenate([k_x, k_l], axis=2)
        v = jnp.concatenate([v_x, v_l], axis=2)
        sim = jnp.einsum('bhid,bhjd->bhij', q, k)
        attn = jax.nn.softmax(sim, axis=-1)
        out = jnp.einsum('bhij,bhjd->bhid', attn, v)
        out = jnp.transpose(out, (0, 2, 1, 3)).reshape(b, m, INNER)
        return out @ Wo

    def _L0_ffn_ref(x, gate_w, bias, up_w, up_b, down_w, down_b, sw_up, sb_up, sw_down, sb_down):
        import jax, jax.numpy as jnp
        import numpy as np
        H = 256
        I = 4 * H
        E = 8
        K = 2
        B, S = (2, 256)
        STD = 0.02 / np.sqrt(H)
        b, s, h = x.shape
        xf = x.reshape(-1, h)
        T = xf.shape[0]
        scores = jax.nn.sigmoid(xf @ gate_w + bias)
        top_scores, top_idx = jax.lax.top_k(scores, K)
        top_scores = top_scores / (jnp.sum(top_scores, axis=-1, keepdims=True) + 1e-06)
        w = jnp.zeros((T, E), dtype=xf.dtype).at[jnp.arange(T)[:, None], top_idx].add(top_scores)
        up = jnp.einsum('th,ehi->tei', xf, up_w) + up_b
        hact = jax.nn.gelu(up, approximate=False)
        eo = jnp.einsum('tei,eih->teh', hact, down_w) + down_b
        combined = jnp.einsum('teh,te->th', eo * 0.1, w)
        shared = (jax.nn.gelu(xf @ sw_up + sb_up, approximate=False) @ sw_down + sb_down) * 0.1
        out = (shared + combined).reshape(b, s, h)
        out = out / (jnp.max(jnp.abs(out), axis=-1, keepdims=True) + 1e-06)
        return out

    def _L1_xattn_ref(query, key, value, Wq, bq, Wk, bk, Wv, bv, Wo, bo):
        import jax, jax.numpy as jnp
        import numpy as np
        EMBED = 256
        HEADS = 16
        HEAD_DIM = EMBED // HEADS
        B, S, D = query.shape
        H, Dh = (HEADS, HEAD_DIM)

        def proj(x, W, b):
            y = jnp.einsum('bsd,ed->bse', x, W) + b
            return y.reshape(B, -1, H, Dh).transpose(0, 2, 1, 3)
        q = proj(query, Wq, bq)
        k = proj(key, Wk, bk)
        v = proj(value, Wv, bv)
        attn = jnp.einsum('bhqd,bhkd->bhqk', q, k) / jnp.sqrt(jnp.float32(Dh))
        attn = jax.nn.softmax(attn, axis=-1)
        out = jnp.einsum('bhqk,bhkd->bhqd', attn, v)
        out = out.transpose(0, 2, 1, 3).reshape(B, -1, D)
        out = jnp.einsum('bsd,ed->bse', out, Wo) + bo
        return out

    def _L1_ffn_ref(hidden_states, sim_matrix, gates, q_proj, k_proj, v_proj, o_proj):
        import jax, jax.numpy as jnp
        import numpy as np
        HIDDEN = 256
        HEAD_DIM = 64
        N_EXPERTS = 16
        MIN_EXPERTS = 2
        B, T = (4, 512)

        def _normalize(x, axis):
            n = jnp.sqrt(jnp.sum(x * x, axis=axis, keepdims=True))
            return x / jnp.maximum(n, 1e-12)

        def _ste(x):
            hard = jax.lax.stop_gradient((x > 0).astype(x.dtype))
            return hard + x - jax.lax.stop_gradient(x)

        def _gating(hidden_states, sim_matrix, gates):
            b, t, c = hidden_states.shape
            flat = hidden_states.reshape(b * t, c)
            logits = _normalize(flat, -1) @ _normalize(sim_matrix, 0) - jax.nn.sigmoid(gates)
            gated = jax.nn.relu(logits)
            mask = _ste(gated)
            inactive = jnp.sum(mask, axis=1) == 0
            _, fb_idx = jax.lax.top_k(logits, MIN_EXPERTS)
            fb = jnp.zeros_like(mask).at[jnp.arange(b * t)[:, None], fb_idx].set(1.0)
            fb_applied = inactive[:, None] & (fb > 0)
            mask = jnp.where(fb_applied, 1.0, mask)
            masked_logits = jnp.where(mask > 0, gated, -jnp.inf)
            return jax.nn.softmax(masked_logits, axis=-1).reshape(b, t, -1)
        b, t, c = hidden_states.shape
        rw = _gating(hidden_states, sim_matrix, gates)
        q = jnp.einsum('bte,bted->btd', rw, jnp.einsum('btc,ecd->bted', hidden_states, q_proj))
        k = jnp.einsum('bte,bted->btd', rw, jnp.einsum('btc,ecd->bted', hidden_states, k_proj))
        v = jnp.einsum('bte,bted->btd', rw, jnp.einsum('btc,ecd->bted', hidden_states, v_proj))
        scale = 1.0 / jnp.sqrt(jnp.asarray(HEAD_DIM, dtype=q.dtype))
        scores = jnp.einsum('bqd,bkd->bqk', q, k) * scale
        causal = jnp.tril(jnp.ones((t, t), dtype=bool))
        scores = jnp.where(causal, scores, -jnp.inf)
        attn = jnp.einsum('bqk,bkd->bqd', jax.nn.softmax(scores, axis=-1), v)
        mixed = attn[:, :, None, :] * rw[..., None]
        return jnp.einsum('bted,edc->btc', mixed, o_proj)
    x = x + jnp.tanh(g_xattn[0]) * _L0_xattn_ref(ctx_1024, _layernorm(x, axis=-1), L0_xattn_gamma_x, L0_xattn_beta_x, L0_xattn_gamma_l, L0_xattn_beta_l, L0_xattn_Wq, L0_xattn_Wkv, L0_xattn_Wo)
    x = x + jnp.tanh(g_ffn[0]) * _L0_ffn_ref(_layernorm(x, axis=-1), L0_ffn_gate_w, L0_ffn_bias, L0_ffn_up_w, L0_ffn_up_b, L0_ffn_down_w, L0_ffn_down_b, L0_ffn_sw_up, L0_ffn_sb_up, L0_ffn_sw_down, L0_ffn_sb_down)
    x = x + jnp.tanh(g_xattn[1]) * _L1_xattn_ref(_layernorm(x, axis=-1), ctx_1024, ctx_1024, L1_xattn_Wq, L1_xattn_bq, L1_xattn_Wk, L1_xattn_bk, L1_xattn_Wv, L1_xattn_bv, L1_xattn_Wo, L1_xattn_bo)
    x = x + jnp.tanh(g_ffn[1]) * _L1_ffn_ref(_layernorm(x, axis=-1), L1_ffn_sim_matrix, L1_ffn_gates, L1_ffn_q_proj, L1_ffn_k_proj, L1_ffn_v_proj, L1_ffn_o_proj)
    return x

_drawn_inputs = setup_inputs


def setup_inputs(seed=0):
    import zlib

    import numpy as np

    out = dict(_drawn_inputs(seed))
    spreads = {'g_ffn': (-1.0, 0.6),
     'L0_xattn_gamma_x': (1.0, 0.2),
     'L0_xattn_beta_x': (0.0, 0.1),
     'L0_xattn_gamma_l': (1.0, 0.2),
     'L0_xattn_beta_l': (0.0, 0.1),
     'L0_ffn_bias': (0.0, 0.1),
     'L0_ffn_up_b': (0.0, 0.578),
     'L0_ffn_down_b': (0.0, 0.1),
     'L0_ffn_sb_up': (0.0, 0.514),
     'L0_ffn_sb_down': (0.0, 0.1),
     'L1_xattn_bq': (0.0, 0.284),
     'L1_xattn_bk': (0.0, 0.8),
     'L1_xattn_bv': (0.0, 0.1),
     'L1_xattn_bo': (0.0, 0.1),
     'L1_ffn_gates': (0.0, 0.1)}
    factors = {'L0_ffn_up_w': 8.0, 'L0_ffn_down_w': 5.302, 'L0_ffn_sw_up': 8.0, 'L0_ffn_sw_down': 8.0}
    for name, (base, spread) in spreads.items():
        noise = np.random.default_rng([zlib.crc32(name.encode()), seed]).standard_normal(out[name].shape)
        drawn = base * np.exp(spread * noise) if base else spread * noise
        out[name] = jnp.asarray(drawn.astype(out[name].dtype))
    for name, factor in factors.items():
        out[name] = (out[name] * factor).astype(out[name].dtype)
    return out
```

```python
from contextlib import ExitStack

import numpy as np

import concourse.bass as bass
from concourse import mybir

F32 = mybir.dt.float32
F32R = mybir.dt.float32r
ALU = mybir.AluOpType
ACT = mybir.ActivationFunctionType
AX = mybir.AxisListType.X

P = 128
B, TQ, D = 8, 112, 256
TK = 375
TOK = B * TQ
NT = TOK // P
KC = D // P
CR = TK // 3
H0, DH0 = 8, 64
NK0 = TK + TQ
KP0 = 122
NKP0 = 4 * KP0
E0, FF = 8, 1024
FM = FF // P
H1, DH1 = 16, 16
E1, DH2 = 16, 64
EPS = 1e-5


def positive(v):
    return not isinstance(v, int) or v > 0


def hold(eng, waits_seen):
    eng.sem_inc(waits_seen, 1)


def build(nc, a, out):
    ctx = ExitStack()
    with ctx:
        def sb(name, shape, dt=F32):
            return ctx.enter_context(nc.sbuf_tensor(name, shape, dt))

        def sem(name):
            return ctx.enter_context(nc.semaphore(name))

        ps = ctx.enter_context(nc.psum_tensor("ps", [P, 8, 512], F32))

        ident = sb("ident", [P, P])
        cos_t = sb("cos_t", [P, NK0])
        sin_t = sb("sin_t", [P, NK0])
        qsign = sb("qsign", [P, 1])
        headmask = sb("headmask", [P, 8])
        iota = sb("iota", [P, 16])
        causal = sb("causal", [TQ, TQ])
        ones = sb("ones", [P, P])
        mhalf = sb("mhalf", [P, 32])
        phalf = sb("phalf", [P, 32])
        x = sb("x", [P, NT, D])
        xn = sb("xn", [P, NT, D])
        xnT = sb("xnT", [P, KC, TOK])
        OT = sb("OT", [P, 4, TOK])
        gate = sb("gate", [P, 4])
        tgate = sb("tgate", [P, 4])
        affine = sb("affine", [P, 4, KC])
        st6 = sb("st6", [P, NT, 6])
        mv = sb("mv", [P, NT, 2])
        veps = sb("veps", [P, NT])
        rstd = sb("rstd", [P, NT])
        negmax = sb("negmax", [P, 4])
        rsum = sb("rsum", [P, 4])
        rinv = sb("rinv", [P, 4])
        wbuf0 = sb("wbuf0", [P, 2 * FM * D])
        hbuf = sb("hbuf", [P, 2, TOK])
        acc = sb("acc", [P, NT, D])
        rt = sb("rt", [P, 14, NT * E0])
        rs1 = sb("rs1", [P, 6, NT])
        wexp = sb("wexp", [P, E0, NT])
        wtok = sb("wtok", [P, NT, E0 + 1])
        wT = sb("wT", [E0 + 1, TOK])
        gw = sb("gw", [P, KC, E0])
        gbias = sb("gbias", [P, E0])
        upb_rows = sb("upb_rows", [(E0 + 1) * FM, P])
        upb = sb("upb", [P, (E0 + 1) * FM])
        dnb = sb("dnb", [E0 + 1, D])
        w1 = sb("w1", [P, 4, KC, D])
        b1 = sb("b1", [P, 2, KC])
        bv = sb("bv", [P, D])
        bo = sb("bo", [P, D])
        simm = sb("simm", [P, KC, E1])
        simsq = sb("simsq", [P, KC, E1])
        gates = sb("gates", [P, E1])
        sgate = sb("sgate", [P, E1])
        rw = sb("rw", [TQ, B, E1])

        st6c = sb("st6c", [CR, 3, 6])
        mvc = sb("mvc", [CR, 3, 2])
        vepsc = sb("vepsc", [CR, 3])
        rstdc = sb("rstdc", [CR, 3])
        n2 = sb("n2", [TQ, B + E1])
        rn2 = sb("rn2", [TQ, B + E1])
        gs = sb("gs", [TQ, 6, B])
        am = sb("am", [TQ, 4])

        ARENA = 27200
        with nc.sbuf_tensor("arena", [P, ARENA], F32) as arena:
            pass
        spare = ExitStack()

        def split_buf(name, shape):
            return spare.enter_context(nc.sbuf_tensor(name, shape, F32R))

        w_hi = [split_buf(f"w_hi{k}", [P, 2 * FM * D]) for k in (0, 1)]
        w_lo = [split_buf(f"w_lo{k}", [P, 2 * FM * D]) for k in (0, 1)]
        x_hi, x_lo = split_buf("x_hi", [P, KC, TOK]), split_buf("x_lo", [P, KC, TOK])
        h_hi, h_lo = split_buf("h_hi", [P, 4, TOK]), split_buf("h_lo", [P, 4, TOK])
        spare.close()


        def layout(start, *shapes):
            views, at = [], start
            for shape in shapes:
                n = int(np.prod(shape[1:]))
                names = " ".join("abcd"[:len(shape) - 1])
                v = arena[0:shape[0], at:at + n].rearrange(
                    f"p ({names}) -> p {names}", **dict(zip("abcd", shape[1:])))
                views.append(v)
                at += n
            assert at <= ARENA, at
            return views

        (wq, wkv, wo, cx_0, cx_1, hat_0, hat_1, kvin_0, kvin_1, kaug_0, kaug_1, v_0, v_1, qa_0, qa_1, probs, pT,
         ) = layout(0, [P, KC, H0, P], [P, KC, 1024], [P, 4, D], [CR, 3, D], [CR, 3, D],
                    [CR, 3, D], [CR, 3, D], [P, KC, NKP0], [P, KC, NKP0], [P, H0, NKP0], [P, H0, NKP0],
                    [KP0, 4, 512], [KP0, 4, 512], [P, H0, TQ], [P, H0, TQ], [TQ, 4, NKP0], [KP0, 2, 4 * TQ])
        cx, hat, kvin, kaug = (cx_0, cx_1), (hat_0, hat_1), (kvin_0, kvin_1), (kaug_0, kaug_1)
        v0, qaug = (v_0, v_1), (qa_0, qa_1)

        (cy_0, cy_1, ctxT_0, ctxT_1, kT_0, kT_1, vm_0, vm_1, qt, qm_0, qm_1, probs1, pT1,
         ) = layout(0, [CR, 3, D], [CR, 3, D], [P, KC, TK], [P, KC, TK], [P, KC, TK], [P, KC, TK],
                    [CR, 3, H1, 32], [CR, 3, H1, 32], [P, KC, TQ], [P, H1, TQ], [P, H1, TQ],
                    [TQ, 4, TK], [CR, 2, 3 * TQ])
        cy, ctxT, kT = (cy_0, cy_1), (ctxT_0, ctxT_1), (kT_0, kT_1)
        vm, qm = (vm_0, vm_1), (qm_0, qm_1)

        (wqkv, wo1) = layout(ARENA - 6144 - 2048, [P, KC, E1, 3 * DH2], [P, E1 * DH2 // P, D])
        (mixT, xsq, xb_0, xb_1, qkv, mix0, mix1, qkT, scm, pr2, pT2, att, mixed, g1,
         ) = layout(0, [P, 8, TOK], [P, KC, TOK], [P, KC, TQ], [P, KC, TQ], [TQ, 2, 192], [TQ, 192], [TQ, 192],
                    [DH2, 2, TQ], [TQ, TQ], [TQ, TQ], [TQ, TQ], [TQ, DH2], [TQ, E1, DH2], [TQ, 16, B * E1])
        xb = (xb_0, xb_1)

        def w_up(w):
            return w[:, 0:FM * D].rearrange("p (c n) -> p c n", c=KC)

        def w_down(w):
            return w[:, FM * D:2 * FM * D].rearrange("p (m n) -> p m n", m=FM)

        s_const, s_x, s_w0, s_small, s_w1, s_wF = (sem(n) for n in (
            "consts_loaded", "x_loaded", "w_l0_loaded", "small_loaded", "w_l1_loaded", "w_l1ffn_loaded"))
        s_cx = [sem("ctx_loaded_even"), sem("ctx_loaded_odd")]
        s_fill = sem("constants_made")
        s_seen = sem("waits_seen")
        s_tanh = sem("gates_tanh")
        s_stat, s_rstd, s_xn = sem("stats_done"), sem("rstd_done"), sem("xn_done")
        s_xt, s_xte = sem("xn_transposed"), sem("xnT_ready")
        s_op = sem("outproj_done")
        s_cst, s_cstat, s_crstd, s_hat, s_lat = (sem(n) for n in (
            "ctx_partial_stats", "ctx_stats", "ctx_rstd", "ctx_normed", "latents_in"))
        s_link_v, s_link_p, s_link_a = sem("vector_chain"), sem("pool_chain"), sem("scalar_chain")

        def ring(tag):
            return {n: sem(f"{tag}_{n}") for n in (
                "t1", "q", "k", "v", "t1e", "qe", "ke", "ve", "s", "max", "exp", "rinv",
                "norm", "pt", "pte", "pv", "ote")}

        L0, L1 = ring("l0"), ring("l1")
        s_qt = sem("l1_q_biased")
        s_rlog = sem("router_logits")
        s_rexp, s_rz = sem("router_exp"), sem("router_z")
        s_route = sem("router_weights")
        s_upbt, s_upbe = sem("upb_transposed"), sem("upb_ready")
        s_wl = sem("expert_w_loaded")
        s_whi, s_wsplit = sem("expert_w_high"), sem("expert_w_split")
        s_xhi, s_xsplit = sem("x_high"), sem("x_split")
        s_hhi, s_hsplit = sem("h_high"), sem("h_split")
        s_up, s_gelu, s_down, s_acc = (sem(n) for n in ("up_done", "gelu_done", "down_done", "acc_done"))
        s_wt, s_wte, s_bias = sem("wT_done"), sem("wT_ready"), sem("bias_mm_done")
        s_gsq, s_gmm, s_gpow, s_gz, s_gexp, s_grw = (sem(n) for n in (
            "squares_ready", "gating_products", "gating_norms", "gating_z", "gating_exp", "gating_ready"))
        s_gsum = sem("gating_sums")
        s_sge, s_sgz = sem("gates_exp"), sem("gates_loaded")
        (s_xb, s_m, s_mx, s_qkv, s_qk, s_qkTe, s_sc, s_scm, s_nm, s_ex, s_ri, s_p2, s_p2e, s_o, s_att, s_mixd, s_mt,
         s_mte) = (sem("f_" + n) for n in (
             "xb", "qkv_products", "mix_step", "qkv_ready", "qk_transposed", "qkT_ready", "scores", "masked", "max",
             "exp", "rinv", "p_transposed", "pT_ready", "o", "att", "mixed", "mix_transposed", "mixT_ready"))
        s_mixg = sem("f_group_used")
        s_out, s_y = sem("out_stored"), sem("y_ready")

        block = ctx.enter_context(nc.Block())

        @block.sync
        def _(sp):
            def ctx_load(n, dst, p):
                sp.dma_start(dst[p], a["ctx"][n, :, :].rearrange("(p t) d -> p t d", t=3)).then_inc(s_cx[p], 16)

            sp.dma_start(x[:, :, :], a["x"].rearrange("b q d -> (b q) d").rearrange("(t p) d -> p t d", p=P)).then_inc(s_x, 16)
            ctx_load(0, cx, 0)
            sp.dma_start(ident[:, :], a["ident"]).then_inc(s_const, 16)
            sp.dma_start(affine[:, :, :].rearrange("p a c -> p (a c)"), a["affine"]).then_inc(s_const, 16)
            sp.dma_start(qsign[:, :], a["qsign"]).then_inc(s_const, 16)
            sp.dma_start(wq, a["wq"].rearrange("(c p) h m -> p c h m", p=P)).then_inc(s_w0, 16)
            sp.dma_start(cos_t[:, :], a["cos"]).then_inc(s_const, 16)
            sp.dma_start(sin_t[:, :], a["sin"]).then_inc(s_const, 16)
            sp.dma_start(wkv, a["wkv"].rearrange("(c p) n -> p c n", p=P)).then_inc(s_w0, 16)
            ctx_load(1, cx, 1)
            sp.dma_start(wo, a["wo"].rearrange("(c p) n -> p c n", p=P)).then_inc(s_w0, 16)
            small = [
                (gate[:, :], a["gate"].rearrange("(a n) -> a n", a=1).broadcast_to([P, 4])),
                (headmask[:, :], a["headmask"]), (iota[:, :], a["iota"]), (causal[:, :], a["causal"]),
                (gw[:, :, :], a["gate_w"].rearrange("(c p) e -> p c e", p=P)),
                (gbias[:, :], a["rbias"].rearrange("(a n) -> a n", a=1).broadcast_to([P, E0])),
                (upb_rows[0:FM, :], a["sb_up"].rearrange("(m p) -> m p", p=P)),
                (upb_rows[FM:, :], a["up_b"].rearrange("e (m p) -> (e m) p", p=P)),
                (dnb[0:E0, :], a["down_b"]),
                (dnb[E0:E0 + 1, :], a["sb_down"].rearrange("(a n) -> a n", a=1)),
                (b1[:, :, :].rearrange("p a c -> p (a c)"), a["bqk"]),
                (bv[:, :], a["bv"].rearrange("(a n) -> a n", a=1).broadcast_to([P, D])),
                (bo[:, :], a["bo"].rearrange("(a n) -> a n", a=1).broadcast_to([P, D])),
                (simm[:, :, :], a["sim"].rearrange("(c p) e -> p c e", p=P)),
                (gates[:, :], a["gates"].rearrange("(a n) -> a n", a=1).broadcast_to([P, E1])),
            ]
            for dst, src in small:
                sp.dma_start(dst, src).then_inc(s_small, 16)
            assert len(small) == N_SMALL
            sp.dma_start(w_up(wbuf0), a["sw_up"].rearrange("(c p) n -> p c n", p=P)).then_inc(s_wl, 16)
            sp.dma_start(w_down(wbuf0), a["sw_down"].rearrange("(m p) n -> p m n", p=P)).then_inc(s_wl, 16)
            for k, name in enumerate(("w1q", "w1k", "w1v", "w1o")):
                sp.dma_start(w1[:, k], a[name].rearrange("(c p) n -> p c n", p=P)).then_inc(s_w1, 16)
            with sp.Fori(0, 3) as i:
                for p in (0, 1):
                    sp.wait_ge(s_hat, i * 2 + p + 1)
                    ctx_load(i * 2 + p + 2, cx, p)
            with sp.Fori(0, E0) as e:
                sp.wait_ge(s_wsplit, e * 8 + 8)
                sp.dma_start(w_up(wbuf0), a["up_w"][e, :, :].rearrange("(c p) n -> p c n", p=P)).then_inc(s_wl, 16)
                sp.dma_start(w_down(wbuf0), a["down_w"][e, :, :].rearrange("(m p) n -> p m n", p=P)).then_inc(s_wl, 16)
            sp.wait_ge(s_down, (E0 + 1) * FM)
            ctx_load(0, cy, 0)
            ctx_load(1, cy, 1)
            sp.dma_start(wqkv, a["wqkv"].rearrange("(c p) e n -> p c e n", p=P)).then_inc(s_wF, 16)
            sp.dma_start(wo1, a["o_proj"].rearrange("(k p) n -> p k n", p=P)).then_inc(s_wF, 16)
            with sp.Fori(0, 3) as i:
                for p in (0, 1):
                    sp.wait_ge(L1["t1"], (i * 2 + p + 1) * KC)
                    ctx_load(i * 2 + p + 2, cy, p)
            for t in range(NT):
                sp.wait_ge(s_y, t + 1)
                sp.dma_start(out.rearrange("b q d -> (b q) d")[t * P:(t + 1) * P, :], x[:, t, :]).then_inc(s_out, 16)
            sp.wait_ge(s_out, 16 * NT)

        @block.gpsimd
        def _(pool):
            pool.memset(ones[:, :], 1.0).then_inc(s_fill, 1)
            pool.memset(mhalf[:, :], -0.5).then_inc(s_fill, 1)
            pool.memset(phalf[:, :], 0.5).then_inc(s_fill, 1)
            pool.memset(kvin_0[:, :, NK0:NKP0], 0.0).then_inc(s_fill, 1)
            pool.memset(kvin_1[:, :, NK0:NKP0], 0.0).then_inc(s_fill, 1)
            pool.memset(probs[:, :, NK0:NKP0], 0.0).then_inc(s_fill, 1)
            pool.memset(wtok[:, :, E0:E0 + 1], 1.0).then_inc(s_fill, 1)
            pool.wait_ge(s_fill, N_FILL)
            chain = [0]

            def link(ins):
                chain[0] += 1
                ins.then_inc(s_link_p, 1)
                pool.wait_ge(s_link_p, chain[0])

            def tile_rstd(k):
                pool.wait_ge(s_stat, k + 1)
                link(pool.tensor_scalar(veps[:, :], mv[:, :, 1], EPS, None, ALU.add))
                pool.tensor_tensor(rstd[:, :], veps[:, :], mhalf[:, 0:NT], ALU.pow).then_inc(s_rstd, 1)

            def ctx_norm(n, p, late=False):
                pool.wait_ge(s_cstat, n + 1)
                hold(pool, s_seen)
                pool.tensor_scalar(vepsc[:, :], mvc[:, :, 1], EPS, None, ALU.add).then_inc(s_crstd, 1)
                pool.wait_ge(s_crstd, 2 * n + 1)
                pool.tensor_tensor(rstdc[:, :], vepsc[:, :], mhalf[0:CR, 0:3], ALU.pow).then_inc(s_crstd, 1)
                pool.wait_ge(s_crstd, 2 * n + 2)
                if positive(n - 1):
                    pool.wait_ge(L0["t1"], (n - 1) * KC)
                hold(pool, s_seen)
                for t in range(3):
                    ins = pool.tensor_scalar(hat[p][:, t, :], cx[p][:, t, :], mvc[:, t, 0:1], rstdc[:, t:t + 1],
                                             ALU.subtract, ALU.mult)
                ins.then_inc(s_hat, 1)

            def latents(n, p):
                if positive(n - 1):
                    pool.wait_ge(L0["v"], (n - 1) * 4)
                pool.tensor_copy(kvin[p][:, :, TK:NK0], xnT[:, :, bass.ds(n * TQ, TQ)]).then_inc(s_lat, 1)

            ctx_norm(0, 0)
            tile_rstd(0)
            tile_rstd(1)
            pool.wait_ge(s_xte, NT)
            latents(0, 0)
            ctx_norm(1, 1)
            latents(1, 1)
            with pool.Fori(0, 3) as i:
                for p in (0, 1):
                    ctx_norm(i * 2 + p + 2, p)
                    latents(i * 2 + p + 2, p)
            tile_rstd(2)
            tile_rstd(3)
            pool.memset(vm_0[:, :, :, :], 0.0).then_inc(s_fill, 1)
            pool.memset(vm_1[:, :, :, :], 0.0).then_inc(s_fill, 1)
            tile_rstd(4)
            pool.wait_ge(s_gsum, 1)
            pool.tensor_tensor(rn2[:, :], n2[:, :], phalf[0:TQ, 0:B + E1], ALU.pow).then_inc(s_gpow, 1)
            def f_rows(n, p):
                if positive(n - 1):
                    pool.wait_ge(s_m, (n - 1) * 8)
                pool.tensor_copy(xb[p], xnT[:, :, bass.ds(n * TQ, TQ)]).then_inc(s_xb, 1)

            f_rows(0, 0)
            f_rows(1, 1)
            with pool.Fori(0, 3) as i:
                f_rows(i * 2 + 2, 0)
                f_rows(i * 2 + 3, 1)

        @block.scalar
        def _(act):
            def xnT_out(k, scale, bias):
                for t in range(NT):
                    act.wait_ge(s_xt, k * NT + t + 1)
                    for c in range(KC):
                        src = ps[:, t, c * P:(c + 1) * P]
                        dst = xnT[:, c, t * P:(t + 1) * P]
                        if scale is None:
                            ins = act.activation(dst, src, ACT.Copy)
                        else:
                            ins = act.activation(dst, src, ACT.Identity, scale=affine[:, scale, c:c + 1],
                                                 bias=affine[:, bias, c:c + 1])
                    ins.then_inc(s_xte, 1)

            act.wait_ge(s_const, 16 * N_CONST)

            def l0_t1(n, p):
                for c in range(KC):
                    act.wait_ge(L0["t1"], n * KC + c + 1)
                    if c == 0 and positive(n - 1):
                        act.wait_ge(L0["v"], (n - 1) * 4)
                    act.activation(kvin[p][:, c, 0:TK], ps[:, 5 + c, 0:TK], ACT.Identity,
                                   scale=affine[:, 0, c:c + 1], bias=affine[:, 1, c:c + 1]).then_inc(L0["t1e"], 1)

            def l0_q(n, p):
                for k in range(2):
                    act.wait_ge(L0["q"], n * 2 + k + 1)
                    if k == 0 and positive(n - 1):
                        act.wait_ge(L0["s"], (n - 1) * H0)
                    bank = (7, 5)[k]
                    act.activation(qaug[p][:, 4 * k:4 * k + 4, :].rearrange("p h q -> p (h q)"),
                                   ps[:, bank, 0:4 * TQ], ACT.Copy, scale=qsign[:, 0:1]).then_inc(L0["qe"], 1)

            def l0_v(n, p, j):
                act.wait_ge(L0["v"], n * 4 + j + 1)
                if j == 0 and positive(n - 1):
                    act.wait_ge(L0["pv"], (n - 1) * H0)
                act.activation(v0[p][:, j, :], ps[0:KP0, L0_BANK["v", j], :], ACT.Copy).then_inc(L0["ve"], 1)

            def l0_exp(n, h):
                g = n * H0 + h
                act.wait_ge(L0["max"], g + 1)
                if positive(g - 3):
                    act.wait_ge(L0["pt"], g - 3)
                act.activation(probs[:, h % 4, 0:NK0], ps[0:TQ, h % 2, 0:NK0], ACT.Exp, bias=negmax[0:TQ, h % 2:h % 2 + 1],
                               accum_out=rsum[0:TQ, h % 4:h % 4 + 1]).then_inc(L0["exp"], 1)

            def l0_pt(g, h):
                act.wait_ge(L0["pt"], g + 1)
                if positive(g - 1):
                    act.wait_ge(L0["pv"], g - 1)
                act.activation(pT[:, h % 2, :], ps[0:KP0, 2 + h % 2, 0:4 * TQ], ACT.Copy).then_inc(L0["pte"], 1)

            def l0_ot(n):
                act.wait_ge(L0["pv"], (n + 1) * H0)
                act.activation(OT[:, :, bass.ds(n * TQ, TQ)], ps[:, 4, 0:4 * TQ].rearrange("p (c q) -> p c q", c=4),
                               ACT.Copy).then_inc(L0["ote"], 1)

            def l0_batch(n, p, nxt):
                for h in range(H0):
                    l0_exp(n, h)
                    if nxt:
                        if h == 2:
                            l0_t1(n + 1, 1 - p)
                        if h == 3:
                            l0_q(n + 1, 1 - p)
                        if h >= 4:
                            l0_v(n + 1, 1 - p, h - 4)
                    if h >= 2 or positive(n):
                        l0_pt(n * H0 + h - 2, (h - 2) % 8)
                    if h == 2 and positive(n):
                        l0_ot(n - 1)

            l0_t1(0, 0)
            xnT_out(0, 2, 3)
            l0_q(0, 0)
            for j in range(4):
                l0_v(0, 0, j)
            l0_batch(0, 0, True)
            with act.Fori(0, 3) as i:
                l0_batch(i * 2 + 1, 1, True)
                l0_batch(i * 2 + 2, 0, True)
            l0_batch(7, 1, False)
            l0_pt(8 * H0 - 2, 6)
            l0_pt(8 * H0 - 1, 7)
            l0_ot(7)
            act.wait_ge(s_small, 16 * N_SMALL)
            act.activation(tgate[:, :], gate[:, :], ACT.Tanh).then_inc(s_tanh, 1)
            act.activation(sgate[:, :], gates[:, :], ACT.Exp, scale=-1.0).then_inc(s_sge, 1)
            act.wait_ge(s_upbt, 1)
            act.activation(upb[:, :], ps[:, 7, 0:(E0 + 1) * FM], ACT.Copy).then_inc(s_upbe, 1)
            xnT_out(1, None, None)
            for j in range(8):
                c = slice(512 * j, 512 * (j + 1))
                act.wait_ge(s_wl, 32)
                act.activation(w_hi[0][:, c], wbuf0[:, c], ACT.Copy).then_inc(s_whi, 1)
            act.wait_ge(s_xte, 2 * NT)
            act.activation(x_hi[:, :, :], xnT[:, :, :], ACT.Copy).then_inc(s_xhi, 1)
            act.wait_ge(s_rz, 1)
            act.activation(rt[:, 1, :], rt[:, 0, :], ACT.Exp, scale=-1.0).then_inc(s_rexp, 1)
            act.wait_ge(s_upbe, 1)

            def split_w(o, k, j):
                if j == 0:
                    act.wait_ge(s_wl, o * 32 + 32)
                c = slice(512 * j, 512 * (j + 1))
                act.activation(w_hi[k][:, c], wbuf0[:, c], ACT.Copy).then_inc(s_whi, 1)

            def gelu(o, m):
                u = o * FM + m
                act.wait_ge(s_up, u + 1)
                if positive(u - 1):
                    act.wait_ge(s_hsplit, u - 1)
                pair = 2 * (m % 2)
                act.activation(hbuf[:, m % 2, :].rearrange("p (a n) -> p a n", a=2), ps[:, pair:pair + 2, 0:TOK // 2],
                               ACT.Gelu, bias=upb[:, bass.ds(u, 1)]).then_inc(s_gelu, 1)
                act.wait_ge(s_gelu, u + 1)
                if positive(u - 3):
                    act.wait_ge(s_down, u - 3)
                act.activation(h_hi[:, m % 4, :], hbuf[:, m % 2, :], ACT.Copy).then_inc(s_hhi, 1)

            def expert(o, k, nxt):
                for m in range(FM):
                    gelu(o, m)
                    if nxt and 2 <= m < 6:
                        if m == 2 and positive(o):
                            act.wait_ge(s_down, o * FM)
                        for j in (2 * m - 4, 2 * m - 3):
                            split_w(o + 1, 1 - k, j)

            expert(0, 0, True)
            with act.Fori(0, 3) as i:
                expert(i * 2 + 1, 1, True)
                expert(i * 2 + 2, 0, True)
            expert(7, 1, True)
            expert(8, 0, False)
            act.wait_ge(s_wt, 1)
            act.activation(wT[:, 0:4 * P], ps[0:E0 + 1, 0, 0:4 * P], ACT.Copy)
            act.activation(wT[:, 4 * P:], ps[0:E0 + 1, 1, 0:TOK - 4 * P], ACT.Copy).then_inc(s_wte, 1)
            xnT_out(2, None, None)

            def l1_t1(n, p):
                for c in range(KC):
                    act.wait_ge(L1["t1"], n * KC + c + 1)
                    if c == 0 and positive(n - 1):
                        act.wait_ge(L1["v"], (n - 1) * 3)
                    act.activation(ctxT[p][:, c, :], ps[:, 5 + c, 0:TK], ACT.Copy).then_inc(L1["t1e"], 1)

            def l1_k(n, p):
                for c in range(KC):
                    act.wait_ge(L1["k"], n * KC + c + 1)
                    if c == 0 and positive(n - 1):
                        act.wait_ge(L1["s"], (n - 1) * H1)
                    act.activation(kT[p][:, c, :], ps[:, (6, 7)[c], 0:TK], ACT.Identity,
                                   bias=b1[:, 1, c:c + 1]).then_inc(L1["ke"], 1)

            def l1_exp(n, h):
                g = n * H1 + h
                act.wait_ge(L1["max"], g + 1)
                if positive(g - 3):
                    act.wait_ge(L1["pt"], g - 3)
                act.activation(probs1[:, h % 4, :], ps[0:TQ, h % 2, 0:TK], ACT.Exp, bias=negmax[0:TQ, h % 2:h % 2 + 1],
                               accum_out=rsum[0:TQ, h % 4:h % 4 + 1]).then_inc(L1["exp"], 1)

            def l1_pt(g, h):
                act.wait_ge(L1["pt"], g + 1)
                if positive(g - 1):
                    act.wait_ge(L1["pv"], g - 1)
                act.activation(pT1[:, h % 2, :], ps[0:CR, 2 + h % 2, 0:3 * TQ], ACT.Copy).then_inc(L1["pte"], 1)

            def l1_ot(n):
                act.wait_ge(L1["pv"], (n + 1) * H1)
                act.activation(OT[:, 0:KC, bass.ds(n * TQ, TQ)], ps[:, 4, 0:KC * TQ].rearrange("p (c q) -> p c q", c=KC),
                               ACT.Copy).then_inc(L1["ote"], 1)

            def l1_batch(n, p, nxt):
                for h in range(H1):
                    l1_exp(n, h)
                    if nxt and h == 2:
                        l1_t1(n + 1, 1 - p)
                    if nxt and h == 6:
                        l1_k(n + 1, 1 - p)
                    if h >= 2 or positive(n):
                        l1_pt(n * H1 + h - 2, (h - 2) % 16)
                    if h == 2 and positive(n):
                        l1_ot(n - 1)

            l1_t1(0, 0)
            l1_k(0, 0)
            l1_batch(0, 0, True)
            with act.Fori(0, 3) as i:
                l1_batch(i * 2 + 1, 1, True)
                l1_batch(i * 2 + 2, 0, True)
            l1_batch(7, 1, False)
            l1_pt(8 * H1 - 2, 14)
            l1_pt(8 * H1 - 1, 15)
            l1_ot(7)
            xnT_out(3, None, None)
            act.wait_ge(s_xte, 4 * NT)
            act.activation(xsq, xnT[:, :, :], ACT.Square).then_inc(s_gsq, 1)
            act.activation(simsq[:, :, :], simm[:, :, :], ACT.Square).then_inc(s_gsq, 1)
            act.wait_ge(s_gz, 1)
            act.activation(g1[:, 2, :], g1[:, 1, :], ACT.Exp).then_inc(s_gexp, 1)

            def f_att(n, p, step):
                if step == 1:
                    act.wait_ge(s_qk, n + 1)
                    act.activation(qkT, ps[0:DH2, 4, 0:2 * TQ].rearrange("p (a q) -> p a q", a=2), ACT.Copy)\
                       .then_inc(s_qkTe, 1)
                if step == 2:
                    act.wait_ge(s_nm, n + 1)
                    act.activation(pr2, scm, ACT.Exp, bias=am[:, 0:1], accum_out=am[:, 1:2]).then_inc(s_ex, 1)
                if step == 4:
                    act.wait_ge(s_p2, n + 1)
                    act.activation(pT2, ps[0:TQ, 6, 0:TQ], ACT.Copy).then_inc(s_p2e, 1)
                if step == 7:
                    act.wait_ge(s_mt, n + 1)
                    act.activation(mixT[:, :, bass.ds(n * TQ, TQ)].rearrange("p (a k) q -> p a k q", a=2),
                                   ps[:, 4:6, 0:4 * TQ].rearrange("p a (k q) -> p a k q", k=4), ACT.Copy)\
                       .then_inc(s_mte, 1)

            with act.Fori(0, 8) as n:
                for s in (1, 2, 4, 7):
                    f_att(n, 0, s)

        @block.vector
        def _(dve):
            chain = [0]

            def link(ins):
                chain[0] += 1
                ins.then_inc(s_link_v, 1)
                dve.wait_ge(s_link_v, chain[0])

            def ctx_stats(n, p):
                dve.wait_ge(s_cx[p], (n // 2 + 1) * 16 if isinstance(n, int) else n * 8 + (8 if p else 16))
                if positive(n):
                    dve.wait_ge(s_hat, n)
                for t in range(3):
                    ins = dve.bn_stats(st6c[:, t, :], cx[p][:, t, :])
                    ins.then_inc(s_cst, 1)
                dve.wait_ge(s_cst, n * 3 + 3)
                hold(dve, s_seen)
                for t in range(3):
                    ins = dve.bn_aggr(mvc[:, t, :], st6c[:, t, :])
                ins.then_inc(s_cstat, 1)

            def tile_stats(src):
                for t in range(NT):
                    ins = dve.bn_stats(st6[:, t, :], src[:, t, :])
                link(ins)
                for t in range(NT):
                    ins = dve.bn_aggr(mv[:, t, :], st6[:, t, :])
                ins.then_inc(s_stat, 1)

            def tile_norm(k, src, last=True):
                dve.wait_ge(s_rstd, k + 1)
                dve.wait_ge(s_stat, k + 1)
                for t in range(NT):
                    ins = dve.tensor_scalar(xn[:, t, :], src[:, t, :], mv[:, t, 0:1], rstd[:, t:t + 1],
                                            ALU.subtract, ALU.mult)
                    if last:
                        ins.then_inc(s_xn, 1)
                if not last:
                    link(ins)

            def residual(k, g, bias):
                dve.wait_ge(s_tanh, 1)
                for t in range(NT):
                    dve.wait_ge(s_op, k * NT + t + 1)
                    src = ps[:, t, 0:D]
                    if bias is not None:
                        link(dve.tensor_tensor(xn[:, t, :], src, bias[:, :], ALU.add))
                        src = xn[:, t, :]
                    ins = dve.scalar_tensor_tensor(x[:, t, :], src, tgate[:, g:g + 1], x[:, t, :], ALU.mult, ALU.add)
                link(ins)

            dve.wait_ge(s_fill, N_FILL)
            ctx_stats(0, 0)
            dve.wait_ge(s_x, 16)
            tile_stats(x)
            tile_norm(0, x, last=False)
            tile_stats(xn)
            tile_norm(1, xn)
            ctx_stats(1, 1)
            dve.wait_ge(s_const, 16 * N_CONST)

            def l0_k(n, p, m):
                dve.wait_ge(L0["k"], n * 4 + m + 1)
                if m == 0 and positive(n - 1):
                    dve.wait_ge(L0["s"], (n - 1) * H0)
                bank = L0_BANK["k", m]
                for half in (0, 1):
                    src = ps[64 * half:64 * half + 64, bank, 0:NK0]
                    h = 2 * m + half
                    dve.tensor_tensor(kaug[p][0:64, h, 0:NK0], src, cos_t[64 * half:64 * half + 64, :], ALU.mult)
                    ins = dve.tensor_tensor(kaug[p][64:128, h, 0:NK0], src, sin_t[64 * half:64 * half + 64, :], ALU.mult)
                ins.then_inc(L0["ke"], 1)

            def softmax_max(L, g, h, n):
                dve.wait_ge(L["s"], g + 1)
                dve.tensor_reduce(negmax[0:TQ, h % 2:h % 2 + 1], ps[0:TQ, h % 2, 0:n], AX, ALU.max, negate=True)\
                   .then_inc(L["max"], 1)

            def softmax_norm(L, g, h, buf, n):
                dve.wait_ge(L["exp"], g + 1)
                r = h % 4
                dve.reciprocal(rinv[0:TQ, r:r + 1], rsum[0:TQ, r:r + 1]).then_inc(L["rinv"], 1)
                dve.wait_ge(L["rinv"], g + 1)
                dve.tensor_scalar(buf[:, r, 0:n], buf[:, r, 0:n], rinv[0:TQ, r:r + 1], None, ALU.mult)\
                   .then_inc(L["norm"], 1)

            def l0_batch(n, p, nxt, stats):
                for h in range(H0):
                    softmax_max(L0, n * H0 + h, h, NK0)
                    if nxt and h >= 4:
                        l0_k(n + 1, 1 - p, h - 4)
                    if h >= 1 or positive(n):
                        softmax_norm(L0, n * H0 + h - 1, (h - 1) % 8, probs, NKP0)
                    if stats and h == 2:
                        ctx_stats(n + 2, p)

            for m in range(4):
                l0_k(0, 0, m)
            l0_batch(0, 0, True, True)
            with dve.Fori(0, 2) as i:
                l0_batch(i * 2 + 1, 1, True, True)
                l0_batch(i * 2 + 2, 0, True, True)
            l0_batch(5, 1, True, True)
            l0_batch(6, 0, True, False)
            l0_batch(7, 1, False, False)
            softmax_norm(L0, 8 * H0 - 1, 7, probs, NKP0)
            residual(0, 0, None)
            tile_stats(x)
            tile_norm(2, x)

            def bc(v, n):
                return v.unsqueeze(2).broadcast_to([v.shape[0], v.shape[1], n])

            def bcm(v, m):
                return v.unsqueeze(1).broadcast_to([v.shape[0], m, v.shape[1]])

            def rv(k):
                return rt[:, k, :].rearrange("p (t e) -> p t e", t=NT)

            def split_w(o, k, j):
                c = slice(512 * j, 512 * (j + 1))
                dve.wait_ge(s_whi, o * 8 + j + 1)
                dve.tensor_tensor(w_lo[k][:, c], wbuf0[:, c], w_hi[k][:, c].bitcast(F32), ALU.subtract)\
                   .then_inc(s_wsplit, 1)

            def split_h(o, m):
                u = o * FM + m
                dve.wait_ge(s_hhi, u + 1)
                dve.tensor_tensor(h_lo[:, m % 4, :], hbuf[:, m % 2, :], h_hi[:, m % 4, :].bitcast(F32), ALU.subtract)\
                   .then_inc(s_hsplit, 1)

            for j in range(8):
                split_w(0, 0, j)
            dve.wait_ge(s_xhi, 1)
            dve.tensor_tensor(x_lo[:, :, :], xnT[:, :, :], x_hi[:, :, :].bitcast(F32), ALU.subtract).then_inc(s_xsplit, 1)
            dve.wait_ge(s_rlog, 1)
            dve.tensor_tensor(rv(0), ps[:, 7, 0:NT * E0].rearrange("p (t e) -> p t e", t=NT),
                              bcm(gbias[:, :], NT), ALU.add).then_inc(s_rz, 1)
            dve.wait_ge(s_rexp, 1)
            link(dve.tensor_scalar(rt[:, 2, :], rt[:, 1, :], 1.0, None, ALU.add))
            link(dve.reciprocal(rt[:, 3, :], rt[:, 2, :]))

            def first_largest(view, m, oh, work, iota_v, top, val, idx):
                link(dve.tensor_reduce(top, view, AX, ALU.max))
                link(dve.tensor_tensor(work, view, bc(top, m), ALU.is_lt))
                link(dve.tensor_scalar(work, work, 1000.0, None, ALU.mult))
                link(dve.tensor_tensor(work, work, iota_v, ALU.add))
                link(dve.tensor_reduce(idx, work, AX, ALU.min))
                link(dve.tensor_tensor(oh, work, bc(idx, m), ALU.is_equal))

            io8 = bcm(iota[:, 0:E0], NT)
            first_largest(rv(3), E0, rv(4), rv(5), io8, rs1[:, 0, :], None, rs1[:, 1, :])
            link(dve.scalar_tensor_tensor(rt[:, 6, :], rt[:, 4, :], -4.0, rt[:, 3, :], ALU.mult, ALU.add))
            first_largest(rv(6), E0, rv(7), rv(8), io8, rs1[:, 2, :], None, rs1[:, 3, :])
            link(dve.tensor_tensor(rs1[:, 4, :], rs1[:, 0, :], rs1[:, 2, :], ALU.add))
            link(dve.tensor_scalar(rs1[:, 4, :], rs1[:, 4, :], 1e-6, None, ALU.add))
            link(dve.reciprocal(rs1[:, 5, :], rs1[:, 4, :]))
            link(dve.tensor_tensor(rt[:, 9, :], rt[:, 4, :], rt[:, 7, :], ALU.add))
            link(dve.tensor_tensor(rt[:, 10, :], rt[:, 9, :], rt[:, 3, :], ALU.mult))
            dve.tensor_tensor(wtok[:, :, 0:E0], rv(10), bc(rs1[:, 5, :], E0), ALU.mult).then_inc(s_route, 1)
            dve.tensor_tensor(wexp[:, :, :].rearrange("p e t -> p t e"), rv(10), bc(rs1[:, 5, :], E0), ALU.mult)\
               .then_inc(s_route, 1)

            def down_src(t):
                return ps[:, 4 + t // 2, (t % 2) * D:(t % 2) * D + D]

            def take(o):
                dve.wait_ge(s_down, o * FM + FM)
                if positive(o):
                    dve.wait_ge(s_acc, o * NT)
                for t in range(NT):
                    if positive(o):
                        ins = dve.scalar_tensor_tensor(
                            acc[:, t, :], down_src(t), wexp[:, bass.ds(o - 1, 1), t:t + 1].rearrange("p a b -> p (a b)"),
                            acc[:, t, :], ALU.mult, ALU.add)
                    else:
                        ins = dve.tensor_copy(acc[:, t, :], down_src(t))
                    ins.then_inc(s_acc, 1)

            def expert(o, k, nxt):
                for m in range(FM):
                    split_h(o, m)
                    if m == 1 and positive(o):
                        take(o - 1)
                    if nxt and 2 <= m < 6:
                        for j in (2 * m - 4, 2 * m - 3):
                            split_w(o + 1, 1 - k, j)

            dve.wait_ge(s_route, 2)
            expert(0, 0, True)
            expert(1, 1, True)
            with dve.Fori(0, 3) as i:
                expert(i * 2 + 2, 0, True)
                expert(i * 2 + 3, 1, True)
            expert(8, 0, False)
            take(8)
            dve.wait_ge(s_acc, (E0 + 1) * NT)
            dve.wait_ge(s_bias, 1)
            for t in range(NT):
                ins = dve.tensor_tensor(acc[:, t, :], acc[:, t, :], down_src(t), ALU.add)
            link(ins)
            link(dve.tensor_scalar(acc[:, :, :], acc[:, :, :], 0.1, None, ALU.mult))
            link(dve.tensor_reduce(rs1[:, 0, :], acc[:, :, :], AX, ALU.max, apply_absolute_value=True))
            link(dve.tensor_scalar(rs1[:, 1, :], rs1[:, 0, :], 1e-6, None, ALU.add))
            link(dve.reciprocal(rs1[:, 2, :], rs1[:, 1, :]))
            link(dve.tensor_tensor(acc[:, :, :], acc[:, :, :], bc(rs1[:, 2, :], D), ALU.mult))
            link(dve.scalar_tensor_tensor(x[:, :, :], acc[:, :, :], tgate[:, 2:3], x[:, :, :], ALU.mult, ALU.add))
            tile_stats(x)
            tile_norm(3, x)

            def l1_q(n, p):
                for c in range(KC):
                    dve.wait_ge(L1["q"], n * KC + c + 1)
                    if positive(n):
                        dve.wait_ge(L1["qe"], n * KC)
                    dve.tensor_scalar(qt[:, c, :], ps[:, (7, 5)[c], 0:TQ], b1[:, 0, c:c + 1], 0.25,
                                      ALU.add, ALU.mult).then_inc(s_qt, 1)
                for c in range(KC):
                    dve.wait_ge(s_qt, n * KC + c + 1)
                    if c == 0 and positive(n - 1):
                        dve.wait_ge(L1["s"], (n - 1) * H1)
                    dve.tensor_tensor(qm[p][:, 8 * c:8 * c + 8, :], bcm(qt[:, c, :], 8), bc(headmask[:, :], TQ),
                                      ALU.mult).then_inc(L1["qe"], 1)

            def l1_v(n, p, j):
                dve.wait_ge(L1["v"], n * 3 + j + 1)
                if j == 0 and positive(n - 1):
                    dve.wait_ge(L1["pv"], (n - 1) * H1)
                src = ps[0:CR, (5, 6, 7)[j], 0:D].rearrange("p (g o d) -> p g o d", o=2, d=DH1)
                bias = bv[0:CR, :].rearrange("p (g o d) -> p g o d", o=2, d=DH1)
                dst = vm[p][:, j].rearrange("p (g o) d -> p g o d", o=2)
                for o in (0, 1):
                    ins = dve.tensor_tensor(dst[:, :, o, 16 * o:16 * o + 16], src[:, :, o, :], bias[:, :, o, :], ALU.add)
                ins.then_inc(L1["ve"], 1)

            def l1_batch(n, p, nxt):
                for h in range(H1):
                    softmax_max(L1, n * H1 + h, h, TK)
                    if nxt and h == 4:
                        l1_q(n + 1, 1 - p)
                    if nxt and h in (8, 10, 12):
                        l1_v(n + 1, 1 - p, (h - 8) // 2)
                    if h >= 1 or positive(n):
                        softmax_norm(L1, n * H1 + h - 1, (h - 1) % 16, probs1, TK)

            dve.wait_ge(s_fill, N_FILL + 2)
            l1_q(0, 0)
            for j in range(3):
                l1_v(0, 0, j)
            l1_batch(0, 0, True)
            with dve.Fori(0, 3) as i:
                l1_batch(i * 2 + 1, 1, True)
                l1_batch(i * 2 + 2, 0, True)
            l1_batch(7, 1, False)
            softmax_norm(L1, 8 * H1 - 1, 15, probs1, TK)
            residual(1, 1, bo)
            tile_stats(x)
            tile_norm(4, x)

            dve.wait_ge(s_gmm, 1)
            link(dve.tensor_copy(n2[:, 0:B], ps[0:TQ, 1, 0:B]))
            dve.tensor_copy(n2[:, B:], ps[0:TQ, 2, 0:E1]).then_inc(s_gsum, 1)
            dve.wait_ge(s_sge, 1)
            link(dve.tensor_scalar(sgate[:, :], sgate[:, :], 1.0, None, ALU.add))
            link(dve.reciprocal(gates[:, :], sgate[:, :]))
            dve.wait_ge(s_gpow, 1)
            link(dve.tensor_scalar(n2[:, :], rn2[:, :], 1e-12, None, ALU.max))
            link(dve.reciprocal(rn2[:, :], n2[:, :]))

            def gv(k):
                return g1[:, k, :].rearrange("p (b e) -> p b e", b=B)

            link(dve.tensor_tensor(gv(0), ps[0:TQ, 0, 0:B * E1].rearrange("p (b e) -> p b e", b=B),
                                   bc(rn2[:, 0:B], E1), ALU.mult))
            link(dve.tensor_tensor(gv(0), gv(0), bcm(rn2[:, B:], B), ALU.mult))
            link(dve.tensor_tensor(gv(0), gv(0), bcm(gates[0:TQ, :], B), ALU.subtract))
            io16 = bcm(iota[0:TQ, :], B)
            first_largest(gv(0), E1, gv(4), gv(5), io16, gs[:, 0, :], None, gs[:, 1, :])
            link(dve.scalar_tensor_tensor(g1[:, 6, :], g1[:, 4, :], -8.0, g1[:, 0, :], ALU.mult, ALU.add))
            first_largest(gv(6), E1, gv(7), gv(8), io16, gs[:, 2, :], None, gs[:, 3, :])
            link(dve.tensor_tensor(g1[:, 9, :], g1[:, 4, :], g1[:, 7, :], ALU.add))
            link(dve.tensor_scalar(gs[:, 4, :], gs[:, 0, :], 0.0, None, ALU.is_le))
            link(dve.tensor_tensor(gv(9), gv(9), bc(gs[:, 4, :], E1), ALU.mult))
            link(dve.tensor_scalar(g1[:, 10, :], g1[:, 0, :], 0.0, None, ALU.is_gt))
            link(dve.tensor_tensor(g1[:, 9, :], g1[:, 9, :], g1[:, 10, :], ALU.add))
            link(dve.tensor_scalar(g1[:, 11, :], g1[:, 0, :], 0.0, None, ALU.max))
            link(dve.tensor_scalar(gs[:, 5, :], gs[:, 0, :], 0.0, None, ALU.max))
            dve.tensor_tensor(gv(1), gv(11), bc(gs[:, 5, :], E1), ALU.subtract).then_inc(s_gz, 1)
            dve.wait_ge(s_gexp, 1)
            link(dve.tensor_tensor(g1[:, 3, :], g1[:, 2, :], g1[:, 9, :], ALU.mult))
            link(dve.tensor_reduce(gs[:, 1, :], gv(3), AX, ALU.add))
            link(dve.reciprocal(gs[:, 2, :], gs[:, 1, :]))
            link(dve.tensor_tensor(rw[:, :, :], gv(3), bc(gs[:, 2, :], E1), ALU.mult))

            def rwe(n, e):
                return rw[:, bass.ds(n, 1), e:e + 1].rearrange("p a b -> p (a b)")

            def f_mix(n, p, g):
                dve.wait_ge(s_m, n * 8 + g + 1)
                if g:
                    dve.wait_ge(s_mx, n * 8 + g)
                for o, m in ((0, mix0), (1, mix1)):
                    src = ps[0:TQ, g % 4, o * 192:o * 192 + 192]
                    if g == 0:
                        if o == 0:
                            if positive(n):
                                dve.wait_ge(s_qkv, n)
                        ins = dve.tensor_scalar(m, src, rwe(n, o), None, ALU.mult)
                    else:
                        ins = dve.scalar_tensor_tensor(m, src, rwe(n, 2 * g + o), m, ALU.mult, ALU.add)
                ins.then_inc(s_mx, 1)
                if g == 7:
                    dve.wait_ge(s_mx, n * 8 + 8)
                    dve.tensor_tensor(qkv[:, p, :], mix0, mix1, ALU.add).then_inc(s_qkv, 1)

            def f_att(n, p, step):
                if step == 2:
                    dve.wait_ge(s_sc, n + 1)
                    dve.scalar_tensor_tensor(scm, ps[0:TQ, 5, 0:TQ], 0.125, causal[:, :], ALU.mult, ALU.add)\
                       .then_inc(s_scm, 1)
                    dve.wait_ge(s_scm, n + 1)
                    dve.tensor_reduce(am[:, 0:1], scm, AX, ALU.max, negate=True).then_inc(s_nm, 1)
                if step == 3:
                    dve.wait_ge(s_ex, n + 1)
                    dve.reciprocal(am[:, 2:3], am[:, 1:2]).then_inc(s_ri, 1)
                if step == 5:
                    dve.wait_ge(s_o, n + 1)
                    dve.wait_ge(s_ri, n + 1)
                    dve.tensor_scalar(att, ps[0:TQ, 7, 0:DH2], am[:, 2:3], None, ALU.mult).then_inc(s_att, 1)
                    dve.wait_ge(s_att, n + 1)
                    dve.tensor_tensor(mixed, bcm(att, E1),
                                      bc(rw[:, bass.ds(n, 1), :].rearrange("p a e -> p (a e)"), DH2), ALU.mult)\
                       .then_inc(s_mixd, 1)

            for g in range(8):
                f_mix(0, 0, g)
            for g in range(8):
                f_mix(1, 1, g)
                f_att(0, 0, g)
            with dve.Fori(0, 3) as i:
                for p in (0, 1):
                    n = i * 2 + 2 + p
                    for g in range(8):
                        f_mix(n, p, g)
                        f_att(n - 1, 1 - p, g)
            for g in range(8):
                f_att(7, 1, g)
            for t in range(NT):
                dve.wait_ge(s_op, 2 * NT + t + 1)
                dve.scalar_tensor_tensor(x[:, t, :], ps[:, t, 0:D], tgate[:, 3:4], x[:, t, :], ALU.mult, ALU.add)\
                   .then_inc(s_y, 1)

        @block.tensor
        def _(pe):
            def T(dst, src, k):
                return pe.transpose(dst, src, ident[0:k, 0:k])

            def xn_T(k, j):
                for t in range(NT):
                    pe.wait_ge(s_xn, j * NT + t + 1)
                    for c in range(KC):
                        ins = T(ps[:, t, c * P:(c + 1) * P], xn[:, t, c * P:(c + 1) * P], P)
                    ins.then_inc(s_xt, 1)

            pe.wait_ge(s_const, 16 * N_CONST)

            def l0_t1(n, p):
                pe.wait_ge(s_hat, n + 1)
                for c in range(KC):
                    l0_bank_free(n, "t1", c)
                    for t in range(3):
                        ins = T(ps[:, 5 + c, t * CR:(t + 1) * CR], hat[p][:, t, c * P:(c + 1) * P], CR)
                    ins.then_inc(L0["t1"], 1)

            def l0_bank_free(n, kind, j):
                evac, count, back = L0_PREV[kind, j]
                if positive(n - back + 1):
                    pe.wait_ge(L0[evac], (n - back) * L0_PER[evac] + count)

            def l0_q(n, p):
                pe.wait_ge(s_lat, n + 1)
                for k in range(2):
                    bank = L0_BANK["q", k]
                    l0_bank_free(n, "q", k)
                    for h in range(4):
                        for c in range(KC):
                            ins = pe.matmul(ps[:, bank, h * TQ:(h + 1) * TQ], wq[:, c, 4 * k + h, :],
                                            kvin[p][:, c, TK:NK0], start=(c == 0), stop=(c == KC - 1))
                    ins.then_inc(L0["q"], 1)

            def l0_kv(n, p, j):
                pe.wait_ge(L0["t1e"], (n + 1) * KC)
                for kind in ("k", "v"):
                    l0_bank_free(n, kind, j)
                    bank = L0_BANK[kind, j]
                    for c in range(KC):
                        if kind == "k":
                            ins = pe.matmul(ps[:, bank, 0:NK0], wkv[:, c, j * P:(j + 1) * P], kvin[p][:, c, 0:NK0],
                                            start=(c == 0), stop=(c == KC - 1))
                        else:
                            ins = pe.matmul(ps[0:KP0, bank, :], kvin[p][:, c, j * KP0:(j + 1) * KP0],
                                            wkv[:, c, 512:1024], start=(c == 0), stop=(c == KC - 1))
                    ins.then_inc(L0[kind], 1)

            def l0_s(n, p, h):
                g = n * H0 + h
                if h == 0:
                    pe.wait_ge(L0["qe"], (n + 1) * 2)
                    pe.wait_ge(L0["ke"], (n + 1) * 4)
                if positive(g - 1):
                    pe.wait_ge(L0["exp"], g - 1)
                pe.matmul(ps[0:TQ, h % 2, 0:NK0], qaug[p][:, h, :], kaug[p][:, h, 0:NK0], start=True, stop=True)\
                  .then_inc(L0["s"], 1)

            def l0_pt(g, h):
                pe.wait_ge(L0["norm"], g + 1)
                if positive(g - 1):
                    pe.wait_ge(L0["pte"], g - 1)
                for j in range(4):
                    ins = T(ps[0:KP0, 2 + h % 2, j * TQ:(j + 1) * TQ], probs[:, h % 4, j * KP0:(j + 1) * KP0], TQ)
                ins.then_inc(L0["pt"], 1)

            def l0_pv(g, h, n, p):
                pe.wait_ge(L0["pte"], g + 1)
                if h == 0:
                    pe.wait_ge(L0["ve"], (n + 1) * 4)
                    if positive(n):
                        pe.wait_ge(L0["ote"], n)
                r = 64 * (h % 2)
                for j in range(4):
                    ins = pe.matmul(ps[r:r + 64, 4, (h // 2) * TQ:(h // 2 + 1) * TQ], v0[p][:, j, h * DH0:(h + 1) * DH0],
                                    pT[:, h % 2, j * TQ:(j + 1) * TQ], start=(j == 0), stop=(j == 3),
                                    tile_position=(0, r))
                ins.then_inc(L0["pv"], 1)

            def l0_batch(n, p, nxt):
                for h in range(H0):
                    l0_s(n, p, h)
                    if nxt:
                        if h == 2:
                            l0_t1(n + 1, 1 - p)
                        if h == 3:
                            l0_q(n + 1, 1 - p)
                        if h >= 4:
                            l0_kv(n + 1, 1 - p, h - 4)
                    if h >= 2 or positive(n):
                        l0_pt(n * H0 + h - 2, (h - 2) % 8)
                    if h >= 3:
                        l0_pv(n * H0 + h - 3, h - 3, n, p)
                    elif positive(n):
                        l0_pv(n * H0 + h - 3, h + 5, n - 1, 1 - p)

            l0_t1(0, 0)
            pe.wait_ge(L0["t1e"], KC)
            xn_T(0, 0)
            pe.wait_ge(s_xte, NT)
            pe.wait_ge(s_w0, 16 * N_W0)
            l0_q(0, 0)
            for j in range(4):
                l0_kv(0, 0, j)
            l0_batch(0, 0, True)
            with pe.Fori(0, 3) as i:
                l0_batch(i * 2 + 1, 1, True)
                l0_batch(i * 2 + 2, 0, True)
            l0_batch(7, 1, False)
            l0_pv(8 * H0 - 3, 5, 7, 1)
            l0_pt(8 * H0 - 2, 6)
            l0_pv(8 * H0 - 2, 6, 7, 1)
            l0_pt(8 * H0 - 1, 7)
            l0_pv(8 * H0 - 1, 7, 7, 1)

            def out_proj(wt, src, chunks, start_bank=0):
                for t in range(NT):
                    for c in range(chunks):
                        ins = pe.matmul(ps[:, t, 0:D], src[:, c, t * P:(t + 1) * P], wt[:, c, :],
                                        start=(c == 0), stop=(c == chunks - 1))
                    ins.then_inc(s_op, 1)

            pe.wait_ge(L0["ote"], B)
            pe.wait_ge(L0["pte"], B * H0)
            pe.wait_ge(L0["ke"], B * 4)
            out_proj(wo, OT, 4)
            pe.wait_ge(s_small, 16 * N_SMALL)
            T(ps[:, 7, 0:(E0 + 1) * FM], upb_rows[:, :], (E0 + 1) * FM).then_inc(s_upbt, 1)
            xn_T(1, 1)
            pe.wait_ge(s_upbe, 1)
            pe.wait_ge(s_xte, 2 * NT)
            for t in range(NT):
                for c in range(KC):
                    ins = pe.matmul(ps[:, 7, t * E0:(t + 1) * E0], xnT[:, c, t * P:(t + 1) * P], gw[:, c, :],
                                    start=(c == 0), stop=(c == KC - 1))
            ins.then_inc(s_rlog, 1)

            def three(dst, lhs, rhs, start, stop):
                (lh, ll), (rh, rl) = lhs, rhs
                pe.matmul(dst, lh, rh, start=start, stop=False, skip_group_check=True)
                pe.matmul(dst, lh, rl, start=False, stop=False, skip_group_check=True)
                return pe.matmul(dst, ll, rh, start=False, stop=stop, skip_group_check=True)

            def up(o, k, m):
                u = o * FM + m
                if m == 0:
                    pe.wait_ge(s_wsplit, o * 8 + 8)
                if positive(u - 1):
                    pe.wait_ge(s_hhi, u - 1)
                for half in range(2):
                    cols = slice(half * (TOK // 2), (half + 1) * (TOK // 2))
                    for c in range(KC):
                        ins = three(ps[:, 2 * (m % 2) + half, 0:TOK // 2],
                                    [w_up(w[k])[:, c, m * P:(m + 1) * P] for w in (w_hi, w_lo)],
                                    [v[:, c, cols] for v in (x_hi, x_lo)], c == 0, c == KC - 1)
                ins.then_inc(s_up, 1)

            def down(o, k, m):
                pe.wait_ge(s_hsplit, o * FM + m + 1)
                if m == 0 and positive(o):
                    pe.wait_ge(s_acc, o * NT)
                for t in range(NT):
                    ins = three(ps[:, 4 + t // 2, (t % 2) * D:(t % 2) * D + D],
                                [v[:, m % 4, t * P:(t + 1) * P] for v in (h_hi, h_lo)],
                                [w_down(w[k])[:, m, :] for w in (w_hi, w_lo)], m == 0 and t % 2 == 0, m == FM - 1)
                ins.then_inc(s_down, 1)

            def expert(o, k):
                for m in range(FM):
                    up(o, k, m)
                    if m >= 2:
                        down(o, k, m - 2)
                    elif positive(o):
                        down(o - 1, 1 - k, m + 6)

            pe.wait_ge(s_xsplit, 1)
            pe.wait_ge(s_rz, 1)
            expert(0, 0)
            expert(1, 1)
            with pe.Fori(0, 3) as i:
                expert(i * 2 + 2, 0)
                expert(i * 2 + 3, 1)
            expert(8, 0)
            down(E0, 0, 6)
            down(E0, 0, 7)
            pe.wait_ge(s_gelu, (E0 + 1) * FM)
            pe.wait_ge(s_route, 2)
            for t in range(NT):
                ins = T(ps[0:E0 + 1, t // 4, (t % 4) * P:(t % 4 + 1) * P], wtok[:, t, :], P)
            ins.then_inc(s_wt, 1)
            pe.wait_ge(s_wte, 1)
            pe.wait_ge(s_acc, (E0 + 1) * NT)
            for t in range(NT):
                ins = pe.matmul(ps[:, 4 + t // 2, (t % 2) * D:(t % 2) * D + D], wT[:, t * P:(t + 1) * P], dnb[:, :],
                                start=True, stop=True)
            ins.then_inc(s_bias, 1)
            xn_T(2, 2)
            pe.wait_ge(s_xte, 3 * NT)

            def l1_t1(n, p):
                pe.wait_ge(s_cx[p], (n // 2 + 5) * 16 if isinstance(n, int) else n * 8 + (8 if p else 16) + 64)
                if positive(n):
                    pe.wait_ge(L1["ve"], n * 3)
                for c in range(KC):
                    for t in range(3):
                        ins = T(ps[:, 5 + c, t * CR:(t + 1) * CR], cy[p][:, t, c * P:(c + 1) * P], CR)
                    ins.then_inc(L1["t1"], 1)

            def l1_q(n, p):
                for k in range(KC):
                    bank = (7, 5)[k]
                    if k == 0:
                        if positive(n):
                            pe.wait_ge(L1["ve"], n * 3)
                    else:
                        pe.wait_ge(L1["t1e"], n * KC + 1)
                    for c in range(KC):
                        ins = pe.matmul(ps[:, bank, 0:TQ], w1[:, 0, c, k * P:(k + 1) * P],
                                        xnT[:, c, bass.ds(n * TQ, TQ)], start=(c == 0), stop=(c == KC - 1))
                    ins.then_inc(L1["q"], 1)

            def l1_k(n, p):
                pe.wait_ge(L1["t1e"], (n + 1) * KC)
                pe.wait_ge(s_qt, n * KC + 1)
                for k in range(KC):
                    for c in range(KC):
                        ins = pe.matmul(ps[:, (6, 7)[k], 0:TK], w1[:, 1, c, k * P:(k + 1) * P], ctxT[p][:, c, :],
                                        start=(c == 0), stop=(c == KC - 1))
                    ins.then_inc(L1["k"], 1)

            def l1_v(n, p, j):
                if j == 0:
                    pe.wait_ge(s_qt, (n + 1) * KC)
                else:
                    pe.wait_ge(L1["ke"], n * KC + j)
                for c in range(KC):
                    ins = pe.matmul(ps[0:CR, (5, 6, 7)[j], 0:D], ctxT[p][:, c, j * CR:(j + 1) * CR], w1[:, 2, c, :],
                                    start=(c == 0), stop=(c == KC - 1))
                ins.then_inc(L1["v"], 1)

            def l1_s(n, p, h):
                g = n * H1 + h
                if h == 0:
                    pe.wait_ge(L1["qe"], (n + 1) * KC)
                    pe.wait_ge(L1["ke"], (n + 1) * KC)
                if positive(g - 1):
                    pe.wait_ge(L1["exp"], g - 1)
                pe.matmul(ps[0:TQ, h % 2, 0:TK], qm[p][:, h, :], kT[p][:, h // 8, :], start=True, stop=True)\
                  .then_inc(L1["s"], 1)

            def l1_pt(g, h):
                pe.wait_ge(L1["norm"], g + 1)
                if positive(g - 1):
                    pe.wait_ge(L1["pte"], g - 1)
                for j in range(3):
                    ins = T(ps[0:CR, 2 + h % 2, j * TQ:(j + 1) * TQ], probs1[:, h % 4, j * CR:(j + 1) * CR], TQ)
                ins.then_inc(L1["pt"], 1)

            def l1_pv(g, h, n, p):
                pe.wait_ge(L1["pte"], g + 1)
                if h == 0:
                    pe.wait_ge(L1["ve"], (n + 1) * 3)
                    if positive(n):
                        pe.wait_ge(L1["ote"], n)
                pair = h // 2
                r, col = 32 * (pair % 4), (pair // 4) * TQ
                for j in range(3):
                    ins = pe.matmul(ps[r:r + 32, 4, col:col + TQ], vm[p][:, j, h, :], pT1[:, h % 2, j * TQ:(j + 1) * TQ],
                                    start=(j == 0 and h % 2 == 0), stop=(j == 2 and h % 2 == 1), tile_position=(0, r))
                ins.then_inc(L1["pv"], 1)

            def l1_batch(n, p, nxt):
                for h in range(H1):
                    l1_s(n, p, h)
                    if nxt:
                        if h == 2:
                            l1_t1(n + 1, 1 - p)
                        if h == 4:
                            l1_q(n + 1, 1 - p)
                        if h == 6:
                            l1_k(n + 1, 1 - p)
                        if h in (8, 10, 12):
                            l1_v(n + 1, 1 - p, (h - 8) // 2)
                    if h >= 2 or positive(n):
                        l1_pt(n * H1 + h - 2, (h - 2) % 16)
                    if h >= 3:
                        l1_pv(n * H1 + h - 3, h - 3, n, p)
                    elif positive(n):
                        l1_pv(n * H1 + h - 3, h + 13, n - 1, 1 - p)

            pe.wait_ge(s_w1, 64)
            l1_t1(0, 0)
            l1_q(0, 0)
            l1_k(0, 0)
            for j in range(3):
                l1_v(0, 0, j)
            l1_batch(0, 0, True)
            with pe.Fori(0, 3) as i:
                l1_batch(i * 2 + 1, 1, True)
                l1_batch(i * 2 + 2, 0, True)
            l1_batch(7, 1, False)
            l1_pv(8 * H1 - 3, 13, 7, 1)
            l1_pt(8 * H1 - 2, 14)
            l1_pv(8 * H1 - 2, 14, 7, 1)
            l1_pt(8 * H1 - 1, 15)
            l1_pv(8 * H1 - 1, 15, 7, 1)
            pe.wait_ge(L1["ote"], B)
            out_proj(w1[:, 3], OT, KC)
            xn_T(3, 3)
            pe.wait_ge(s_xte, 4 * NT)
            pe.wait_ge(s_gsq, 2)

            for b in range(B):
                for c in range(KC):
                    pe.matmul(ps[0:TQ, 0, b * E1:(b + 1) * E1], xnT[:, c, b * TQ:(b + 1) * TQ], simm[:, c, :],
                              start=(c == 0), stop=(c == KC - 1))
                for c in range(KC):
                    pe.matmul(ps[0:TQ, 1, b:b + 1], xsq[:, c, b * TQ:(b + 1) * TQ], ones[:, 0:1],
                              start=(c == 0), stop=(c == KC - 1))
            for c in range(KC):
                ins = pe.matmul(ps[0:TQ, 2, 0:E1], ones[:, 0:TQ], simsq[:, c, :], start=(c == 0), stop=(c == KC - 1))
            ins.then_inc(s_gmm, 1)
            pe.wait_ge(s_wF, 32)

            def f_qkv(n, p, g):
                if g == 0:
                    pe.wait_ge(s_xb, n + 1)
                    if isinstance(n, int) and n == 0:
                        pe.wait_ge(s_gz, 1)
                if positive(n * 8 + g - 3):
                    pe.wait_ge(s_mx, n * 8 + g - 3)
                for c in range(KC):
                    ins = pe.matmul(ps[0:TQ, g % 4, 0:384], xb[p][:, c, :],
                                    wqkv[:, c, 2 * g:2 * g + 2, :].rearrange("p e n -> p (e n)"),
                                    start=(c == 0), stop=(c == KC - 1))
                ins.then_inc(s_m, 1)

            def f_att(n, p, step):
                if step == 1:
                    pe.wait_ge(s_qkv, n + 1)
                    if positive(n):
                        pe.wait_ge(s_mte, n)
                    hold(pe, s_seen)
                    T(ps[0:DH2, 4, 0:TQ], qkv[:, p, 0:64], TQ)
                    T(ps[0:DH2, 4, TQ:2 * TQ], qkv[:, p, 64:128], TQ).then_inc(s_qk, 1)
                if step == 2:
                    pe.wait_ge(s_qkTe, n + 1)
                    pe.matmul(ps[0:TQ, 5, 0:TQ], qkT[:, 0, :], qkT[:, 1, :], start=True, stop=True).then_inc(s_sc, 1)
                if step == 4:
                    pe.wait_ge(s_ex, n + 1)
                    T(ps[0:TQ, 6, 0:TQ], pr2, TQ).then_inc(s_p2, 1)
                if step == 5:
                    pe.wait_ge(s_p2e, n + 1)
                    pe.matmul(ps[0:TQ, 7, 0:DH2], pT2, qkv[:, p, 128:192], start=True, stop=True).then_inc(s_o, 1)
                if step == 7:
                    pe.wait_ge(s_mixd, n + 1)
                    for k in range(8):
                        ins = T(ps[:, 4 + k // 4, (k % 4) * TQ:(k % 4 + 1) * TQ],
                                mixed[:, 2 * k:2 * k + 2, :].rearrange("p e d -> p (e d)"), TQ)
                    ins.then_inc(s_mt, 1)

            for g in range(8):
                f_qkv(0, 0, g)
            for g in range(8):
                f_qkv(1, 1, g)
                f_att(0, 0, g)
            with pe.Fori(0, 3) as i:
                for p in (0, 1):
                    n = i * 2 + 2 + p
                    for g in range(8):
                        f_qkv(n, p, g)
                        f_att(n - 1, 1 - p, g)
            for g in range(8):
                f_att(7, 1, g)
            pe.wait_ge(s_mte, B)
            pe.wait_ge(s_mx, 64)
            pe.wait_ge(s_att, B)
            out_proj(wo1, mixT, 8)


N_CONST, N_W0, N_SMALL, N_FILL = 5, 3, 15, 7
L0_ORDER = [("t1", 0), ("t1", 1), ("q", 0), ("q", 1), ("k", 0), ("v", 0), ("k", 1), ("v", 1), ("k", 2), ("v", 2),
            ("k", 3), ("v", 3)]
L0_BANK = {job: 5 + j % 3 for j, job in enumerate(L0_ORDER)}
L0_PREV = {job: (L0_ORDER[j - 3][0] + "e", L0_ORDER[j - 3][1] + 1, int(j < 3)) for j, job in enumerate(L0_ORDER)}
L0_PER = {"t1e": 2, "qe": 2, "ke": 4, "ve": 4}


def constants():
    c = {"ident": np.eye(P, dtype=np.float32)}
    inv = (1.0 / np.float32(10000.0) ** (np.arange(0, DH0, 2, dtype=np.float32) / np.float32(DH0))).astype(np.float32)
    pos = (3 * np.arange(CR)[None, :] + np.arange(3)[:, None]).reshape(-1).astype(np.float32)
    angle = (pos[None, :] * inv[np.arange(P) % 32][:, None]).astype(np.float32)
    c["cos"] = np.concatenate([np.cos(angle), np.ones((P, TQ), np.float32)], 1).astype(np.float32)
    c["sin"] = np.concatenate([np.sin(angle), np.zeros((P, TQ), np.float32)], 1).astype(np.float32)
    sign = np.full((P, 1), 0.125, np.float32)
    sign[96:] = -0.125
    c["qsign"] = sign
    c["headmask"] = (np.arange(P)[:, None] // DH1 == np.arange(8)[None, :]).astype(np.float32)
    c["iota"] = np.tile(np.arange(16, dtype=np.float32), (P, 1))
    c["causal"] = np.where(np.arange(TQ)[None, :] <= np.arange(TQ)[:, None], 0.0, -3e38).astype(np.float32)
    return c


def kernel(**inputs):
    import concourse.bacc as bacc
    from concourse.bass_utils import run_bass_kernel_spmd

    i = {k: np.asarray(v) for k, v in inputs.items()}

    def chunks(v):
        return v.reshape(KC, P).T

    wq = i["L0_xattn_Wq"].reshape(D, H0, DH0)
    arrays = {
        "x": i["x"], "ctx": i["ctx_1024"], "gate": np.concatenate([i["g_xattn"], i["g_ffn"]]),
        "wq": np.concatenate([wq, wq[:, :, 32:], wq[:, :, :32]], axis=2),
        "wkv": i["L0_xattn_Wkv"], "wo": i["L0_xattn_Wo"],
        "affine": np.concatenate([chunks(i["L0_xattn_" + n]) for n in ("gamma_x", "beta_x", "gamma_l", "beta_l")], 1),
        "gate_w": i["L0_ffn_gate_w"], "rbias": i["L0_ffn_bias"], "up_w": i["L0_ffn_up_w"], "up_b": i["L0_ffn_up_b"],
        "down_w": i["L0_ffn_down_w"], "down_b": i["L0_ffn_down_b"], "sw_up": i["L0_ffn_sw_up"],
        "sb_up": i["L0_ffn_sb_up"], "sw_down": i["L0_ffn_sw_down"], "sb_down": i["L0_ffn_sb_down"],
        "w1q": i["L1_xattn_Wq"].T, "w1k": i["L1_xattn_Wk"].T, "w1v": i["L1_xattn_Wv"].T, "w1o": i["L1_xattn_Wo"].T,
        "bqk": np.concatenate([chunks(i["L1_xattn_bq"]), chunks(i["L1_xattn_bk"])], 1),
        "bv": i["L1_xattn_bv"], "bo": i["L1_xattn_bo"], "sim": i["L1_ffn_sim_matrix"], "gates": i["L1_ffn_gates"],
        "wqkv": np.concatenate([i["L1_ffn_q_proj"], i["L1_ffn_k_proj"], i["L1_ffn_v_proj"]], 2).transpose(1, 0, 2),
        "o_proj": i["L1_ffn_o_proj"].reshape(E1 * DH2, D),
    }
    arrays.update(constants())
    arrays = {k: np.ascontiguousarray(v) for k, v in arrays.items()}
    nc = bacc.Bacc("TRN2", target_bir_lowering=False, num_devices=1)
    aps = {k: nc.dram_tensor("in_" + k, v.shape, mybir.dt.from_np(v.dtype), kind="ExternalInput").ap()
           for k, v in arrays.items()}
    out = nc.dram_tensor("out", (B, TQ, D), F32, kind="ExternalOutput").ap()
    build(nc, aps, out)
    r = run_bass_kernel_spmd(nc, [{"in_" + k: v for k, v in arrays.items()}], core_ids=[0])
    return r.results[0]["out"]
```
